# Optimizing a Trainium2 kernel written in Bass

```python
import numpy as np
import jax
import jax.numpy as jnp

def _softmax(x, axis=-1):
    return jax.nn.softmax(x, axis=axis)

def _gelu(x):
    return jax.nn.gelu(x, approximate=True)

def _silu(x):
    return jax.nn.silu(x)

def _sigmoid(x):
    return jax.nn.sigmoid(x)

def _layernorm(x, axis=-1, eps=1e-05):
    m = jnp.mean(x, axis=axis, keepdims=True)
    v = jnp.var(x, axis=axis, keepdims=True)
    return (x - m) / jnp.sqrt(v + eps)

def _scatter_add(tgt, idx, src, axis=0):
    return tgt.at[idx].add(src)

def _segment_sum(src, seg, n):
    return jax.ops.segment_sum(src, seg, n)
kernel_name = 'mk_vit_tower_d1_tok_img1024_r4_d15db9'

def setup_inputs(seed: int=0):
    np.random.seed(seed)
    _w = jnp.asarray

    def _rec_inputs():
        import jax
        import jax.numpy as jnp
        _rk = jax.random.key(seed)
        x = jax.random.uniform(jax.random.fold_in(_rk, 1), (64, 3, 256, 256), jnp.float32, 0.0, 1)
        return x
    x = _rec_inputs()

    def _L0_tok_setup():
        import jax, jax.numpy as jnp
        import numpy as np
        _GRAY_W = (0.2989, 0.587, 0.114)
        key = jax.random.key(seed)
        x = jax.random.uniform(key, (32, 3, 256, 256), dtype=jnp.float32)
        sx = jnp.array([[-3.0, 0.0, 3.0], [-10.0, 0.0, 10.0], [-3.0, 0.0, 3.0]], dtype=jnp.float32)
        scharr = jnp.stack([sx, sx.T])[:, None, :, :]
        return {'x': x, 'scharr': scharr}
    _L0_tok_all = _L0_tok_setup()
    _L0_tok_in = {k: v for k, v in _L0_tok_all.items() if k in ('scharr',)}
    del _L0_tok_all

    def _L0_attn_setup():
        import jax, jax.numpy as jnp
        import numpy as np
        B, T, HID = (4, 512, 256)
        NH = 4
        KD, VD = (128, 256)
        DK, DV = (KD // NH, VD // NH)
        R = 32
        GLR = 64
        EPS = 1e-05

        def _rwkv6_scan(r, k, v, w, u):

            def step(S, xs):
                r_t, k_t, v_t, w_t = xs
                kv = k_t[..., :, None] * v_t[..., None, :]
                o_t = jnp.einsum('bhk,bhkv->bhv', r_t, S + u[None, :, :, None] * kv)
                S = jnp.exp(w_t)[..., None] * S + kv
                return (S, o_t)
            S0 = jnp.zeros(r.shape[:2] + (r.shape[-1], v.shape[-1]), r.dtype)
            mv = lambda x: jnp.moveaxis(x, 2, 0)
            _, o = jax.lax.scan(step, S0, (mv(r), mv(k), mv(v), mv(w)))
            return jnp.moveaxis(o, 0, 2)
        key = jax.random.key(seed)
        ks = jax.random.split(key, 20)
        g = lambda i, shape, s=0.02: jax.random.normal(ks[i], shape, dtype=jnp.float32) * s
        return {'hidden_states': jax.random.normal(ks[0], (B, T, HID), dtype=jnp.float32), 'mu0': g(1, (HID,), 0.1), 'W_x0': g(2, (5 * R, HID)), 'W_x2': g(3, (HID, 5 * R)), 'x_bias': g(4, (5, HID), 0.1), 'W_r': g(5, (KD, HID)), 'W_w1': g(6, (GLR, HID)), 'W_w2': g(7, (KD, GLR)), 'b_w2': g(8, (KD,), 0.1), 'W_k': g(9, (KD, HID)), 'W_v': g(10, (VD, HID)), 'W_g': g(11, (VD, HID)), 'bonus': g(12, (NH, DK), 0.1), 'gn_weight': jnp.ones((VD,), jnp.float32) + g(13, (VD,), 0.05), 'gn_bias': g(14, (VD,), 0.05), 'W_o': g(15, (HID, VD))}
    _L0_attn_all = _L0_attn_setup()
    _L0_attn_in = {k: v for k, v in _L0_attn_all.items() if k in ('mu0', 'W_x0', 'W_x2', 'x_bias', 'W_r', 'W_w1', 'W_w2', 'b_w2', 'W_k', 'W_v', 'W_g', 'bonus', 'gn_weight', 'gn_bias', 'W_o')}
    del _L0_attn_all

    def _L0_ffn_setup():
        import jax, jax.numpy as jnp
        import numpy as np
        CAPACITY_FACTOR = 0.5
        NUM_HEADS = 16
        key = jax.random.key(seed)
        ks = jax.random.split(key, 6)
        B, N, D = (4, 1024, 256)
        s = 1.0 / np.sqrt(D)
        return {'token_inputs': jax.random.normal(ks[0], (B, N, D), jnp.float32), 'Wg': jax.random.normal(ks[1], (D, 1), jnp.float32) * s, 'Wq': jax.random.normal(ks[2], (D, D), jnp.float32) * s, 'Wk': jax.random.normal(ks[3], (D, D), jnp.float32) * s, 'Wv': jax.random.normal(ks[4], (D, D), jnp.float32) * s, 'Wo': jax.random.normal(ks[5], (D, D), jnp.float32) * s}
    _L0_ffn_all = _L0_ffn_setup()
    _L0_ffn_in = {k: v for k, v in _L0_ffn_all.items() if k in ('Wg', 'Wq', 'Wk', 'Wv', 'Wo')}
    del _L0_ffn_all
    return {'x': x, 'L0_tok_scharr': _L0_tok_in['scharr'], 'L0_attn_mu0': _L0_attn_in['mu0'], 'L0_attn_W_x0': _L0_attn_in['W_x0'], 'L0_attn_W_x2': _L0_attn_in['W_x2'], 'L0_attn_x_bias': _L0_attn_in['x_bias'], 'L0_attn_W_r': _L0_attn_in['W_r'], 'L0_attn_W_w1': _L0_attn_in['W_w1'], 'L0_attn_W_w2': _L0_attn_in['W_w2'], 'L0_attn_b_w2': _L0_attn_in['b_w2'], 'L0_attn_W_k': _L0_attn_in['W_k'], 'L0_attn_W_v': _L0_attn_in['W_v'], 'L0_attn_W_g': _L0_attn_in['W_g'], 'L0_attn_bonus': _L0_attn_in['bonus'], 'L0_attn_gn_weight': _L0_attn_in['gn_weight'], 'L0_attn_gn_bias': _L0_attn_in['gn_bias'], 'L0_attn_W_o': _L0_attn_in['W_o'], 'L0_ffn_Wg': _L0_ffn_in['Wg'], 'L0_ffn_Wq': _L0_ffn_in['Wq'], 'L0_ffn_Wk': _L0_ffn_in['Wk'], 'L0_ffn_Wv': _L0_ffn_in['Wv'], 'L0_ffn_Wo': _L0_ffn_in['Wo']}

def reference(x, L0_tok_scharr, L0_attn_mu0, L0_attn_W_x0, L0_attn_W_x2, L0_attn_x_bias, L0_attn_W_r, L0_attn_W_w1, L0_attn_W_w2, L0_attn_b_w2, L0_attn_W_k, L0_attn_W_v, L0_attn_W_g, L0_attn_bonus, L0_attn_gn_weight, L0_attn_gn_bias, L0_attn_W_o, L0_ffn_Wg, L0_ffn_Wq, L0_ffn_Wk, L0_ffn_Wv, L0_ffn_Wo):
    import jax
    import jax.numpy as jnp

    def _L0_tok_ref(x, scharr):
        import jax, jax.numpy as jnp
        import numpy as np
        _GRAY_W = (0.2989, 0.587, 0.114)
        w = jnp.asarray(_GRAY_W, dtype=x.dtype)
        gray = jnp.einsum('bchw,c->bhw', x, w)[:, None]
        edges = jax.lax.conv_general_dilated(gray, scharr, window_strides=(1, 1), padding='SAME', dimension_numbers=('NCHW', 'OIHW', 'NCHW'))
        abs_edges = jnp.sqrt(jnp.square(edges))
        edge = abs_edges.sum(axis=1) / 2
        return edge

    def _L0_attn_ref(hidden_states, mu0, W_x0, W_x2, x_bias, W_r, W_w1, W_w2, b_w2, W_k, W_v, W_g, bonus, gn_weight, gn_bias, W_o):
        import jax, jax.numpy as jnp
        import numpy as np
        B, T, HID = (4, 512, 256)
        NH = 4
        KD, VD = (128, 256)
        DK, DV = (KD // NH, VD // NH)
        R = 32
        GLR = 64
        EPS = 1e-05

        def _rwkv6_scan(r, k, v, w, u):

            def step(S, xs):
                r_t, k_t, v_t, w_t = xs
                kv = k_t[..., :, None] * v_t[..., None, :]
                o_t = jnp.einsum('bhk,bhkv->bhv', r_t, S + u[None, :, :, None] * kv)
                S = jnp.exp(w_t)[..., None] * S + kv
                return (S, o_t)
            S0 = jnp.zeros(r.shape[:2] + (r.shape[-1], v.shape[-1]), r.dtype)
            mv = lambda x: jnp.moveaxis(x, 2, 0)
            _, o = jax.lax.scan(step, S0, (mv(r), mv(k), mv(v), mv(w)))
            return jnp.moveaxis(o, 0, 2)
        x = hidden_states
        shifted = jnp.pad(x, ((0, 0), (1, 0), (0, 0)))[:, :-1]
        delta = shifted - x
        xp = jnp.tanh((x + delta * mu0) @ W_x0.T)
        xp = xp.reshape(x.shape[0], x.shape[1], 5, R)
        mus = jnp.einsum('blnr,hnr->blnh', xp, W_x2.reshape(HID, 5, R)) + x_bias
        mu_r, mu_w, mu_k, mu_v, mu_g = (mus[:, :, i] for i in range(5))
        r = (x + delta * mu_r) @ W_r.T
        w = jnp.tanh((x + delta * mu_w) @ W_w1.T) @ W_w2.T + b_w2
        k = (x + delta * mu_k) @ W_k.T
        v = (x + delta * mu_v) @ W_v.T
        g = (x + delta * mu_g) @ W_g.T
        split = lambda t, d: t.reshape(t.shape[0], t.shape[1], NH, d).transpose(0, 2, 1, 3)
        r_, k_, w_ = (split(r, DK), split(k, DK), split(w, DK))
        v_ = split(v, DV)
        w_ = -jnp.exp(w_)
        o = _rwkv6_scan(r_, k_, v_, w_, bonus)
        o = o.transpose(0, 2, 1, 3)
        mean = o.mean(-1, keepdims=True)
        var = o.var(-1, keepdims=True)
        o = (o - mean) * jax.lax.rsqrt(var + EPS)
        o = o.reshape(x.shape[0], x.shape[1], VD) * gn_weight + gn_bias
        o = o * jax.nn.silu(g)
        return o @ W_o.T

    def _L0_ffn_ref(token_inputs, Wg, Wq, Wk, Wv, Wo):
        import jax, jax.numpy as jnp
        import numpy as np
        CAPACITY_FACTOR = 0.5
        NUM_HEADS = 16
        B, N, D = token_inputs.shape
        C = int(N * CAPACITY_FACTOR)
        H = NUM_HEADS
        dh = D // H
        gate = jax.nn.sigmoid((token_inputs @ Wg)[..., 0])
        _, idx = jax.lax.top_k(gate, C)
        attn_in = jnp.take_along_axis(token_inputs, idx[..., None], axis=1)
        q = (attn_in @ Wq).reshape(B, C, H, dh)
        k = (attn_in @ Wk).reshape(B, C, H, dh)
        v = (attn_in @ Wv).reshape(B, C, H, dh)
        scores = jnp.einsum('bqhd,bkhd->bhqk', q, k) / jnp.sqrt(jnp.float32(dh))
        attn = jax.nn.softmax(scores, axis=-1)
        o = jnp.einsum('bhqk,bkhd->bqhd', attn, v).reshape(B, C, D) @ Wo
        gate_sel = jnp.take_along_axis(gate, idx, axis=1)
        out = jnp.zeros_like(token_inputs)
        out = out.at[jnp.arange(B)[:, None], idx].set(o * gate_sel[..., None])
        return out
    h = _L0_tok_ref(x, L0_tok_scharr)
    h = h + _L0_attn_ref(_layernorm(h, axis=-1), L0_attn_mu0, L0_attn_W_x0, L0_attn_W_x2, L0_attn_x_bias, L0_attn_W_r, L0_attn_W_w1, L0_attn_W_w2, L0_attn_b_w2, L0_attn_W_k, L0_attn_W_v, L0_attn_W_g, L0_attn_bonus, L0_attn_gn_weight, L0_attn_gn_bias, L0_attn_W_o)
    h = h + _L0_ffn_ref(_layernorm(h, axis=-1), L0_ffn_Wg, L0_ffn_Wq, L0_ffn_Wk, L0_ffn_Wv, L0_ffn_Wo)
    return h

_drawn_inputs = setup_inputs


def setup_inputs(seed=0):
    import zlib

    import numpy as np

    out = dict(_drawn_inputs(seed))
    spreads = {}
    factors = {'L0_attn_mu0': 8.0,
     'L0_attn_W_x0': 8.0,
     'L0_attn_W_x2': 8.0,
     'L0_attn_x_bias': 8.0,
     'L0_attn_W_r': 2.867,
     'L0_attn_W_w1': 8.0,
     'L0_attn_W_w2': 8.0,
     'L0_attn_b_w2': 8.0,
     'L0_attn_W_k': 2.873,
     'L0_attn_W_v': 2.866,
     'L0_attn_W_g': 2.872,
     'L0_attn_bonus': 8.0,
     'L0_attn_gn_weight': 8.0,
     'L0_attn_gn_bias': 8.0,
     'L0_attn_W_o': 2.86,
     'L0_ffn_Wq': 2.774,
     'L0_ffn_Wk': 2.764}
    for name, (base, spread) in spreads.items():
        noise = np.random.default_rng([zlib.crc32(name.encode()), seed]).standard_normal(out[name].shape)
        drawn = base * np.exp(spread * noise) if base else spread * noise
        out[name] = jnp.asarray(drawn.astype(out[name].dtype))
    for name, factor in factors.items():
        out[name] = (out[name] * factor).astype(out[name].dtype)
    return out
```

```python
import numpy as np
import concourse.bass as bass
import concourse.mybir as mybir
from contextlib import ExitStack
from collections import namedtuple

F32, BF16, I32 = mybir.dt.float32, mybir.dt.bfloat16, mybir.dt.int32
ALU, ACT, AX = mybir.AluOpType, mybir.ActivationFunctionType, mybir.AxisListType

P = 128
T = 256
D = 256
IMG = 2
NT = IMG * T // P
N = IMG * T
FC = D // P
R = 32
NMIX = 5
NH, DK, DV = 4, 32, 64
GLR = 64
EPS = 1e-5
GRAY = (0.2989, 0.587, 0.114)
LEVELS = 7
MASKED = 5
HF, DH, C = 16, 16, 128
SAT_HI, SAT_LO = 16.6355, -88.7
QG = HF // 4

Unit = namedtuple("Unit", "i per first")


def back(u, n):
    return Unit(u.i, u.per, u.first - n)


def exists(u, n=0):
    return u.i is not None or u.first - n >= 0


def scaled(u, per_unit, k):
    const = u.first * per_unit + k
    return const if u.i is None else u.i * (u.per * per_unit) + const


class Event:

    def __init__(self, ctx, nc, name, per_unit=1, by=1):
        self.sem, self.per_unit, self.by = ctx.enter_context(nc.semaphore(name)), per_unit, by

    def done(self, u, k=None):
        return self.sem, scaled(u, self.per_unit * self.by, (self.per_unit if k is None else k) * self.by)


class Slots:

    def __init__(self, ctx, nc, name, per_unit):
        self.per_unit = per_unit
        self.banks = [ctx.enter_context(nc.psum_tensor(f"{name}_psum{b}", [P, 512], F32)) for b in range(2)]
        self.full = [ctx.enter_context(nc.semaphore(f"{name}_full{b}")) for b in range(2)]
        self.free = [ctx.enter_context(nc.semaphore(f"{name}_free{b}")) for b in range(2)]

    def which(self, u, k):
        return (u.first * self.per_unit + k) % 2

    def count(self, u, k, more):
        c = (u.first * self.per_unit + k) // 2 + more
        return c if u.i is None else u.i * (u.per * self.per_unit // 2) + c

    def bank(self, u, k):
        return self.banks[self.which(u, k)]

    def reused(self, u, k):
        return u.i is not None or u.first * self.per_unit + k >= 2

    def emptied(self, u, k):
        return self.free[self.which(u, k)], self.count(u, k, 0)

    def filled(self, u, k):
        return self.full[self.which(u, k)], self.count(u, k, 1)

    def drained(self, u, k):
        return self.free[self.which(u, k)], self.count(u, k, 1)

    def fill(self, u, k):
        return self.full[self.which(u, k)]

    def drain(self, u, k):
        return self.free[self.which(u, k)]


def view(t, offset, dims):
    a = t[:]
    return bass.AP(tensor=a.tensor, offset=a.offset + offset, ap=[list(a.ap[0])] + [list(d) for d in dims])


F_EDGE = lambda r, o: 2 * r + o
F_TR = lambda f: 4 + f
FRONT_SLOTS = 6
M_LOW = lambda n: n
M_MUS = {0: 2, 1: 4, 2: 7, 3: 10, 4: 14}
M_R, M_W1, M_W2, M_K, M_V, M_G = 6, 9, 12, 13, 16, 18
MIX_SLOTS = 20
S_DIAG = 0
S_LEVEL = lambda lv, img: 1 + IMG * lv + img
S_AV = lambda img: 17 + img
S_TR = lambda f: 19 + f
S_OUT = lambda img: 21 + img
SCAN_SLOTS = 23
D_KEY, D_RANK, D_PICK, D_SEL, D_Q, D_K, D_V = range(7)


def depth_slots():
    at, slots = 7, {}
    for n in range(IMG * QG):
        names = [("score", n)]
        if n == QG + 1:
            names.append(("av", 0))
        if n:
            names.append(("turn", n - 1))
        for name in names:
            slots[name] = at
            at += 1
    for name in (("turn", IMG * QG - 1), ("av", 1), "o_turn", "y", ("scatter", 0), ("scatter", 1)):
        slots[name] = at
        at += 1
    return slots, at


D_SLOT, DEPTH_SLOTS = depth_slots()

FRONT, MIX, SCAN, DEPTH = range(4)
STEP = [
    (DEPTH, "key"), (MIX, "low"), (SCAN, "diag"), (DEPTH, "rank"), (MIX, "mus0"), (MIX, "mus1"), (DEPTH, "pick"), (SCAN, "level0"),
    (FRONT, "gray"), (DEPTH, "select"), (SCAN, "level1"), (DEPTH, "qkv"), (DEPTH, "heads0"), (MIX, "r"), (DEPTH, "heads1"), (MIX, "mus2"),
    (SCAN, "level2"), (DEPTH, "heads2"), (MIX, "w1"), (SCAN, "level3"), (MIX, "mus3"), (DEPTH, "heads3"), (SCAN, "level4"),
    (FRONT, "edge0"), (DEPTH, "heads4"), (SCAN, "level5"), (MIX, "w2"), (DEPTH, "heads5"), (SCAN, "level6"), (MIX, "k"), (SCAN, "level7"),
    (DEPTH, "heads6"), (SCAN, "av"), (SCAN, "gnorm"), (DEPTH, "heads7"), (FRONT, "edge1"), (DEPTH, "heads8"), (SCAN, "o_turn"),
    (MIX, "mus4"), (FRONT, "norm"), (DEPTH, "heads9"), (SCAN, "out"), (MIX, "v"), (FRONT, "turn"), (DEPTH, "o_turn"), (SCAN, "norm"),
    (MIX, "g0"), (DEPTH, "y"), (MIX, "g1"), (MIX, "shift"), (SCAN, "spread"), (DEPTH, "scatter"),
]

AHEAD = {(MIX, "shift"), (SCAN, "spread")}


def run_steps(eng, units, stages):
    last = units + 3
    start = 4
    turns = max(0, (units - start) // 2 - 1)

    def step(i, per, first):
        for stream, name in STEP:
            u = Unit(i, per, first - stream + ((stream, name) in AHEAD))
            inside = i is not None or 0 <= u.first < units
            if inside and (stream, name) in stages:
                stages[stream, name](u)

    for s in range(min(start, last)):
        step(None, 0, s)
    if turns:
        with eng.Fori(0, turns) as i:
            step(i, 2, start)
            step(i, 2, start + 1)
    for s in range(start + 2 * turns if turns else min(start, last), last):
        step(None, 0, s)


def build(nc, a, units):
    with ExitStack() as ctx:
        def sb(name, shape, dt=F32):
            return ctx.enter_context(nc.sbuf_tensor(name, shape, dt))

        def event(name, per_unit=1, by=1):
            return Event(ctx, nc, name, per_unit, by)

        ident = sb("ident", [P, P])
        edge_hot = sb("edge_hot", [3, 2, P])
        masks = sb("masks", [P, MASKED, 64], I32)
        earlier = sb("earlier", [P, 2, T])
        slot_no = sb("slot_no", [P, 1])
        head_of = sb("head_of", [P, NH])
        parity = sb("parity", [P, 2])
        taps = sb("taps", [P, 18])
        taps_dx = sb("taps_dx", [3, 6])
        band = sb("band", [P, 6, P])
        halo_w = sb("halo_w", [3, 4, P])
        w_x0 = sb("w_x0", [P, FC, NMIX * R])
        w_x2 = sb("w_x2", [P, NMIX - 1, D])
        w_x2g = sb("w_x2g", [P, D])
        vecs = sb("vecs", [P, 2 + 10 + 1 + 1 + 2 + 2])
        w_r = sb("w_r", [P, FC, P])
        w_w1 = sb("w_w1", [P, FC, GLR])
        w_w2 = sb("w_w2", [GLR, P])
        w_k = sb("w_k", [P, FC, P])
        w_v = sb("w_v", [P, FC, D])
        w_g = sb("w_g", [P, FC, D])
        w_o = sb("w_o", [P, FC, D])
        f_g = sb("f_g", [P, D])
        f_q = sb("f_q", [P, FC, D])
        f_k = sb("f_k", [P, FC, D])
        f_v = sb("f_v", [P, FC, D])
        f_o = sb("f_o", [P, FC, D])
        gn_half = sb("gn_half", [P, 4])
        v_mean = sb("v_mean", [P, FC * NH])
        ones_bf = sb("ones_bf", [P, P], BF16)
        marks = sb("marks", [P, 2 + MASKED * IMG])
        minus_half, eps = sb("minus_half", [P, 8]), sb("eps", [P, 8])
        mu0 = lambda f: vecs[:, f:f + 1]
        x_bias = lambda i, f: vecs[:, 2 + 2 * i + f:3 + 2 * i + f]
        b_w2, bonus = vecs[:, 12:13], vecs[:, 13:14]
        half_gn_w = lambda f: gn_half[:, f:f + 1]
        half_gn_b = lambda f: gn_half[:, 2 + f:3 + f]

        x_in = sb("x_in", [P, 3, IMG, 2, D])
        gray = sb("gray", [P, IMG, 2, D + 2])
        halo = sb("halo", [3, 2, IMG, D])
        h = [sb(f"h{b}", [P, NT, D]) for b in range(2)]
        stats1, mv1, rstd1 = sb("stats1", [P, NT, 6]), sb("mv1", [P, NT, 2]), sb("rstd1", [P, 2, NT])
        xn = sb("xn", [P, NT, D])
        xT = [sb(f"xT{b}", [P, FC, IMG, T + 1]) for b in range(2)]
        h_keep = [sb(f"h_keep{b}", [P, NT, D]) for b in range(2)]
        delta = sb("delta", [P, FC, N])
        low = sb("low", [P, N])
        low_g = sb("low_g", [P, N])
        mixed = [sb(f"mixed{b}", [P, FC, N]) for b in range(2)]
        xp = mixed[1]
        shift3 = low[:, 0:3 * P].rearrange("p (d m) -> p d m", d=3)
        rk = [sb(f"rk{b}", [P, 2, N]) for b in range(2)]
        decay = [sb(f"decay{b}", [P, N]) for b in range(2)]
        v = [sb(f"v{b}", [P, NT, D]) for b in range(2)]
        g_silu = [sb(f"g_silu{b}", [P, FC, N]) for b in range(2)]
        r_heads = sb("r_heads", [P, NH, N])
        diag = sb("diag", [P, NT * NH])
        totals = sb("totals", [P, N])
        A = sb("A", [P, NT * NH, P])
        A_far = sb("A_far", [P, IMG * NH, P])
        o_var = sb("o_var", [P, 3, NT * NH])
        o_n = sb("o_n", [P, NT, D])
        oT = sb("oT", [P, FC, N])
        ruk = oT[:, 0]
        o_sq = oT
        h2 = [sb(f"h2_{b}", [P, NT, D]) for b in range(2)]
        stats2, mv2, rstd2 = sb("stats2", [P, NT, 6]), sb("mv2", [P, NT, 2]), sb("rstd2", [P, 2, NT])
        xn2 = [sb(f"xn2_{b}", [P, NT, D]) for b in range(2)]
        logit = sb("logit", [P, NT])
        key = [sb(f"key{b}", [P, NT]) for b in range(2)]
        gate_e = sb("gate_e", [P, 2, NT])
        gate = [sb(f"gate{b}", [P, NT]) for b in range(2)]
        before = sb("before", [P, NT, T], BF16)
        tie = sb("tie", [P, NT, T], BF16)
        slot_of = sb("slot_of", [P, N])
        pick = sb("pick", [P, NT, C])
        selT = sb("selT", [P, FC, IMG * C])
        q_par = [sb(f"q_par{n}", [P, FC, IMG * C]) for n in range(2)]
        kT = sb("kT", [P, FC, IMG * C])
        vA = sb("vA", [P, IMG * HF, DH + 1])
        peak = sb("peak", [P, 2, 4])
        E = [sb(f"E{b}", [P, 4, C]) for b in range(2)]
        AT = sb("AT", [P, HF, C])
        r_sum = sb("r_sum", [P, HF])
        o_att = sb("o_att", [P, IMG, D])
        o_attT = sb("o_attT", [P, FC, IMG * C])
        y = pick[:].rearrange("p (i j) s -> p i (j s)", i=IMG)
        w_low = pick[0:GLR].rearrange("p j s -> p (j s)")

        front = Slots(ctx, nc, "front", FRONT_SLOTS)
        mix = Slots(ctx, nc, "mix", MIX_SLOTS)
        scan = Slots(ctx, nc, "scan", SCAN_SLOTS)
        depth = Slots(ctx, nc, "depth", DEPTH_SLOTS)

        consts = ctx.enter_context(nc.semaphore("consts_loaded"))
        ready = ctx.enter_context(nc.semaphore("weights_ready"))
        zeroed = ctx.enter_context(nc.semaphore("pads_zeroed"))
        prep = ctx.enter_context(nc.semaphore("weights_step"))
        x_loaded = event("x_loaded", 3 * IMG, 16)
        gray_red, gray_green, gray_ready = event("gray_red"), event("gray_green"), event("gray_ready")
        halo_ready = event("halo_ready", 2 * IMG, 16)
        stats1_ready, mv1_ready, var1_ready, rstd1_ready = (event(n) for n in ("stats1_ready", "mv1_ready", "var1_ready", "rstd1_ready"))
        h_ready, xn_ready = event("h_ready", 2), event("xn_ready")
        h_kept, delta_ready, xp_ready = event("h_kept"), event("delta_ready"), event("xp_ready")
        mixed_ready = event("mixed_ready", NMIX * FC)
        decay_ready = event("decay_ready")
        g_tanh_ready = event("g_tanh_ready", FC)
        ruk_ready = event("ruk_ready")
        r_heads_ready = event("r_heads_ready")
        totals_ready = event("totals_ready", LEVELS - 1)
        diag_set = event("diag_set", IMG)
        decayed = event("decayed", LEVELS)
        o_sq_ready, o_sum_ready, o_var_ready, o_rstd_ready = (event(n, IMG) for n in ("o_sq_ready", "o_sum_ready", "o_var_ready", "o_rstd_ready"))
        oT_ready = event("oT_ready", FC)
        stats2_ready, mv2_ready, var2_ready, rstd2_ready = (event(n) for n in ("stats2_ready", "mv2_ready", "var2_ready", "rstd2_ready"))
        xn2_ready = event("xn2_ready")
        logit_ready, key_ready, gate_exp, gate_sum, gate_ready = (
            event(n) for n in ("logit_ready", "key_ready", "gate_exp", "gate_sum", "gate_ready"))
        tie_ready = event("tie_ready")
        peak_ready, exp_ready = event("peak_ready", IMG * QG), event("exp_ready", IMG * QG)
        sum_ready = event("sum_ready", IMG)
        stored = event("stored", IMG, 16)

        CONST_LOADS = [
            (ident[:], "ident"), (shift3, "shift3"), (edge_hot[:], "edge_hot"), (masks[:], "masks"), (earlier[:], "earlier"),
            (slot_no[:], "slot_no"), (head_of[:], "head_of"), (parity[:], "parity"), (taps[:], "taps"), (taps_dx[:], "taps_dx"),
            (w_x0[:], "w_x0"), (w_x2[:], "w_x2"), (w_x2g[:], "w_x2g"), (vecs[:], "vecs"), (w_r[:], "w_r"), (w_w1[:], "w_w1"),
            (w_w2[:], "w_w2"), (w_k[:], "w_k"), (w_v[:], "w_v"), (w_g[:], "w_g"), (w_o[:], "w_o"), (f_g[:], "f_g"), (f_q[:], "f_q"),
            (f_k[:], "f_k"), (f_v[:], "f_v"), (f_o[:], "f_o")]
        ALL_CONSTS = 16 * len(CONST_LOADS)
        PADS = 10

        def sel(u, pair):
            return pair[u.first % 2]

        def h_rows(u, r):
            return view(sel(u, h), r * D, [[2 * D, IMG], [1, D]])

        def image(u, img):
            return scaled(u, IMG, img)

        block = ctx.enter_context(nc.Block())

        @block.sync
        def _(sp):
            def load(u):
                for c in range(3):
                    for img in range(IMG):
                        sp.dma_start(x_in[:, c, img], a["x"][image(u, img), c].rearrange("(r p) w -> p r w", p=P)).then_inc(x_loaded.sem, 16)

            def gray_stage(u):
                sp.wait_ge(*gray_ready.done(u))
                for img in range(IMG):
                    for side, (p, r) in enumerate(((P - 1, 0), (0, 1))):
                        edge_row = gray[p:p + 1, img, r, 0:1]
                        taps_of = bass.AP(tensor=edge_row.tensor, offset=edge_row.offset, ap=[[list(gray[:].ap[0])[0], 1], [1, 3], [1, D]])
                        sp.dma_start(halo[:, side, img], taps_of).then_inc(halo_ready.sem, 16)
                nxt = back(u, -1)
                if u.i is not None or nxt.first < units:
                    load(nxt)

            def scatter(u):
                for img in range(IMG):
                    sp.wait_ge(*depth.drained(u, D_SLOT["scatter", img]))
                    sp.dma_start(a["out"][image(u, img)].rearrange("(r p) w -> p r w", p=P), sel(u, h2)[:, 2 * img:2 * img + 2]).then_inc(stored.sem, 16)

            for dst, name in CONST_LOADS:
                sp.dma_start(dst, a[name]).then_inc(consts, 16)
            load(Unit(None, 0, 0))
            run_steps(sp, units, {(FRONT, "gray"): gray_stage, (DEPTH, "scatter"): scatter})
            sp.wait_ge(stored.sem, units * IMG * 16)

        @block.gpsimd
        def _(pool):
            g = nc.gpsimd
            g.memset(gray[:, :, :, 0:1], 0.0).then_inc(zeroed, 1)
            g.memset(gray[:, :, :, D + 1:D + 2], 0.0).then_inc(zeroed, 1)
            for b in range(2):
                g.memset(xT[b][:, :, :, 0:1], 0.0).then_inc(zeroed, 1)
            g.memset(vA[:, :, DH:DH + 1], 1.0).then_inc(zeroed, 1)
            g.memset(ones_bf[:], 1.0).then_inc(zeroed, 1)
            g.memset(minus_half[:], -0.5).then_inc(zeroed, 1)
            g.memset(eps[:], EPS).then_inc(zeroed, 1)
            g.memset(low_g[:], 0.0).then_inc(zeroed, 1)
            g.memset(totals[:], 1.0).then_inc(zeroed, 1)
            pool.wait_ge(zeroed, PADS)
            pool.wait_ge(consts, ALL_CONSTS)

            def rstd(u, mv, mv_ready, out, var_ready, rstd_ready):
                pool.wait_ge(*mv_ready.done(u))
                g.tensor_tensor(out[:, 0], mv[:, :, 1], eps[:, 0:NT], ALU.add).then_inc(var_ready.sem, 1)
                pool.wait_ge(*var_ready.done(u))
                g.tensor_tensor(out[:, 1], out[:, 0], minus_half[:, 0:NT], ALU.pow).then_inc(rstd_ready.sem, 1)

            def shift(u):
                for f in range(FC):
                    pool.wait_ge(*front.drained(u, F_TR(f)))
                if exists(u, 1):
                    pool.wait_ge(*mix.drained(back(u, 1), M_MUS[4] + 1))
                x = sel(u, xT)
                g.tensor_tensor(delta[:].rearrange("p f (i t) -> p f i t", i=IMG), x[:, :, :, 0:T], x[:, :, :, 1:T + 1],
                                ALU.subtract).then_inc(delta_ready.sem, 1)

            def mus(i):
                def stage(u):
                    for f in range(FC):
                        pool.wait_ge(*mix.drained(u, M_MUS[i] + f))
                        m = mixed[i % 2][:, f].rearrange("p (i t) -> p i t", i=IMG)
                        g.tensor_tensor(m, m, sel(u, xT)[:, f, :, 1:T + 1], ALU.add).then_inc(mixed_ready.sem, 1)
                return stage

            def diag_stage(u):
                pool.wait_ge(*decay_ready.done(u))
                if exists(u, 1):
                    pool.wait_ge(*decayed.done(back(u, 1)))
                for lv in range(LEVELS - 1):
                    n = N >> (lv + 1)
                    src, at = (sel(u, decay), 0) if lv == 0 else (totals, N - (N >> (lv - 1)))
                    if lv:
                        pool.wait_ge(*totals_ready.done(u, lv))
                    g.tensor_tensor(view(totals, N - (N >> lv), [[1, n]]), view(src, at, [[2, n]]), view(src, at + 1, [[2, n]]),
                                    ALU.mult).then_inc(totals_ready.sem, 1)
                pool.wait_ge(*scan.drained(u, S_DIAG))
                for img in range(IMG):
                    n = NT * NH // IMG
                    g.tensor_tensor(A[:, img * n:(img + 1) * n], view(ident, 0, [[0, n], [1, P]]), view(diag, img * n, [[1, n], [0, P]]),
                                    ALU.mult).then_inc(diag_set.sem, 1)

            def gnorm(u):
                for img in range(IMG):
                    n = NT * NH // IMG
                    at = slice(img * n, (img + 1) * n)
                    pool.wait_ge(*o_sum_ready.done(u, img + 1))
                    g.tensor_tensor(o_var[:, 1, at], o_var[:, 0, at], eps[:, 0:n], ALU.add).then_inc(o_var_ready.sem, 1)
                    pool.wait_ge(*o_var_ready.done(u, img + 1))
                    g.tensor_tensor(o_var[:, 2, at], o_var[:, 1, at], minus_half[:, 0:n], ALU.pow).then_inc(o_rstd_ready.sem, 1)

            stages = {
                (FRONT, "norm"): lambda u: rstd(u, mv1, mv1_ready, rstd1, var1_ready, rstd1_ready),
                (MIX, "shift"): shift,
                (SCAN, "diag"): diag_stage,
                (SCAN, "gnorm"): gnorm,
                (SCAN, "norm"): lambda u: rstd(u, mv2, mv2_ready, rstd2, var2_ready, rstd2_ready),
            }
            for i in range(NMIX):
                stages[MIX, f"mus{i}"] = mus(i)
            run_steps(pool, units, stages)

        @block.scalar
        def _(act):
            s = nc.scalar
            def copy(u, slots, k, out, src=None, func=ACT.Copy, **kw):
                act.wait_ge(*slots.filled(u, k))
                s.activation(out, slots.bank(u, k)[:] if src is None else src, func, **kw).then_inc(slots.drain(u, k), 1)

            def gray_stage(u):
                act.wait_ge(*x_loaded.done(u))
                if exists(u, 1):
                    act.wait_ge(*front.filled(back(u, 1), F_EDGE(1, 1)))
                s.activation(view(gray, 1, [[D + 2, NT], [1, D]]), view(x_in, 0, [[D, NT], [1, D]]), ACT.Copy,
                             scale=GRAY[0]).then_inc(gray_red.sem, 1)

            def edge(r):
                def stage(u):
                    if exists(u, 2):
                        act.wait_ge(*h_kept.done(back(u, 2)))
                        act.wait_ge(*xn_ready.done(back(u, 2)))
                    copy(u, front, F_EDGE(r, 0), h_rows(u, r), front.bank(u, F_EDGE(r, 0))[:].rearrange("p (i d) -> p i d", i=IMG), func=ACT.Abs)
                    copy(u, front, F_EDGE(r, 1), xn[:, 2 * r:2 * r + 2].rearrange("p j d -> p (j d)"), func=ACT.Abs)
                return stage

            def front_turn(u):
                if exists(u, 2):
                    act.wait_ge(*mixed_ready.done(back(u, 2)))
                for f in range(FC):
                    copy(u, front, F_TR(f), sel(u, xT)[:, f, :, 1:T + 1], front.bank(u, F_TR(f))[:].rearrange("p (i t) -> p i t", i=IMG))

            def low_stage(u):
                act.wait_ge(*h_ready.done(u))
                if exists(u, 2):
                    act.wait_ge(*scan.drained(back(u, 2), S_OUT(1)))
                s.activation(sel(u, h_keep)[:], sel(u, h)[:], ACT.Copy).then_inc(h_kept.sem, 1)
                copy(u, mix, M_LOW(0), low[:], func=ACT.Tanh)
                copy(u, mix, M_LOW(1), low_g[0:R], mix.bank(u, M_LOW(1))[0:R, :], func=ACT.Tanh)

            def rk_stage(n, k):
                def stage(u):
                    copy(u, mix, k, sel(u, rk)[:, n])
                return stage

            def w1(u):
                if exists(u, 3):
                    act.wait_ge(*depth.filled(back(u, 3), D_SLOT["scatter", 1]))
                copy(u, mix, M_W1, w_low, mix.bank(u, M_W1)[0:GLR, :], func=ACT.Tanh)

            def w2(u):
                if exists(u, 2):
                    act.wait_ge(*decayed.done(back(u, 2)))
                    act.wait_ge(*totals_ready.done(back(u, 2)))
                copy(u, mix, M_W2, sel(u, decay)[:], func=ACT.Exp, bias=b_w2)
                act.wait_ge(*mix.drained(u, M_W2))
                s.activation(sel(u, decay)[:], sel(u, decay)[:], ACT.Exp, scale=-1.0).then_inc(decay_ready.sem, 1)

            def v_stage(u):
                for n in range(2):
                    copy(u, mix, M_V + n, sel(u, v)[:, 2 * n:2 * n + 2].rearrange("p j d -> p (j d)"))

            def g_stage(f):
                def stage(u):
                    act.wait_ge(*mix.filled(u, M_G + f))
                    if exists(u, 2):
                        act.wait_ge(*oT_ready.done(back(u, 2)))
                    s.activation(sel(u, g_silu)[:, f], mix.bank(u, M_G + f)[:], ACT.Tanh, scale=0.5).then_inc(g_tanh_ready.sem, 1)
                return stage

            def diag_stage(u):
                if exists(u, 1):
                    act.wait_ge(*diag_set.done(back(u, 1)))
                copy(u, scan, S_DIAG, diag[:], scan.bank(u, S_DIAG)[:, 0:NT * NH])

            def spread(u):
                act.wait_ge(*mix.drained(u, M_R))
                if exists(u, 1):
                    act.wait_ge(*scan.filled(back(u, 1), S_LEVEL(LEVELS, IMG - 1)))
                for hh in range(NH):
                    last = s.activation(r_heads[:, hh], sel(u, rk)[:, 0], ACT.Copy, scale=head_of[:, hh:hh + 1])
                last.then_inc(r_heads_ready.sem, 1)

            def level(lv):
                H = 1 << lv

                def stage(u):
                    for img in range(IMG):
                        k = S_LEVEL(lv, img)
                        if lv == LEVELS:
                            copy(u, scan, k, A_far[:, img * NH:(img + 1) * NH].rearrange("p h t -> p (h t)"))
                            continue
                        act.wait_ge(*scan.filled(u, k))
                        act.wait_ge(*diag_set.done(u, img + 1))
                        n = NT * NH // IMG
                        out = A[:, img * n:(img + 1) * n]
                        src = scan.bank(u, k)[:].rearrange("p (n t) -> p n t", n=n)
                        for b in range(64 // H):
                            left, right = slice(2 * H * b, 2 * H * b + H), slice(2 * H * b + H, 2 * H * (b + 1))
                            last = s.activation(out[left, :, right], src[left, :, H * b:H * (b + 1)], ACT.Copy)
                        last.then_inc(scan.drain(u, k), 1)
                return stage

            def gnorm(u):
                for img in range(IMG):
                    act.wait_ge(*scan.filled(u, S_AV(img)))
                    s.activation(o_sq[:, img], scan.bank(u, S_AV(img))[:], ACT.Square,
                                 scale=DV ** -0.5).then_inc(o_sq_ready.sem, 1)

            def scan_turn(u):
                act.wait_ge(*o_sum_ready.done(u))
                for f in range(FC):
                    copy(u, scan, S_TR(f), oT[:, f], func=ACT.Identity, scale=half_gn_w(f), bias=half_gn_b(f))

            def scan_norm(u):
                act.wait_ge(*key_ready.done(u))
                if exists(u, 1):
                    act.wait_ge(*gate_sum.done(back(u, 1)))
                s.activation(gate_e[:, 0], sel(u, key)[:], ACT.Exp, scale=-1.0).then_inc(gate_exp.sem, 1)

            def pick_stage(u):
                copy(u, depth, D_PICK, pick[:].rearrange("p j s -> p (j s)"))

            def select(u):
                copy(u, depth, D_SEL, selT[:].rearrange("p c s -> p (c s)"))

            def qkv(u):
                act.wait_ge(*depth.filled(u, D_Q))
                for n in range(2):
                    last = s.activation(q_par[n][:].rearrange("p c s -> p (c s)"), depth.bank(u, D_Q)[:], ACT.Identity, scale=parity[:, n:n + 1])
                last.then_inc(depth.drain(u, D_Q), 1)
                copy(u, depth, D_K, kT[:].rearrange("p c s -> p (c s)"))
                copy(u, depth, D_V, vA[:, :, 0:DH], depth.bank(u, D_V)[:].rearrange("p (h d) -> p h d", d=DH))

            def heads(n):
                def stage(u):
                    if n < IMG * QG:
                        act.wait_ge(*depth.drained(u, D_SLOT["score", n]))
                        s.activation(E[n % 2][:], E[n % 2][:], ACT.Exp).then_inc(exp_ready.sem, 1)
                    m = n - 1
                    if 0 <= m < IMG * QG and m % 2 == 0:
                        copy(u, depth, D_SLOT["turn", m], AT[:, 4 * (m % QG):4 * (m % QG) + 4], depth.bank(u, D_SLOT["turn", m])[:].rearrange("p (h q) -> p h q", h=4))
                return stage

            def depth_turn(u):
                copy(u, depth, D_SLOT["o_turn"], o_attT[:].rearrange("p c s -> p (c s)"))

            def y_stage(u):
                copy(u, depth, D_SLOT["y"], pick[:].rearrange("p j s -> p (j s)"))

            stages = {
                (FRONT, "gray"): gray_stage, (FRONT, "edge0"): edge(0), (FRONT, "edge1"): edge(1), (FRONT, "turn"): front_turn,
                (MIX, "low"): low_stage, (MIX, "r"): rk_stage(0, M_R), (MIX, "k"): rk_stage(1, M_K), (MIX, "w1"): w1, (MIX, "w2"): w2,
                (MIX, "v"): v_stage, (MIX, "g0"): g_stage(0), (MIX, "g1"): g_stage(1),
                (SCAN, "spread"): spread, (SCAN, "diag"): diag_stage, (SCAN, "gnorm"): gnorm, (SCAN, "o_turn"): scan_turn,
                (SCAN, "norm"): scan_norm, (DEPTH, "pick"): pick_stage, (DEPTH, "select"): select, (DEPTH, "qkv"): qkv, (DEPTH, "o_turn"): depth_turn,
                (DEPTH, "y"): y_stage,
            }
            for lv in range(MASKED, LEVELS + 1):
                stages[SCAN, f"level{lv}"] = level(lv)
            for n in range(IMG * QG + 1):
                stages[DEPTH, f"heads{n}"] = heads(n)
            act.wait_ge(consts, ALL_CONSTS)
            act.wait_ge(zeroed, PADS)
            act.wait_ge(ready, 1)
            run_steps(act, units, stages)

        @block.vector
        def _(dve):
            w = nc.vector
            step = [0]

            def then(ins):
                step[0] += 1
                ins.then_inc(prep, 1)
                dve.wait_ge(prep, step[0])

            dve.wait_ge(consts, ALL_CONSTS)
            dve.wait_ge(zeroed, PADS)
            then(w.tensor_scalar(taps[:], taps[:], 0.5, None, ALU.mult))
            then(w.tensor_scalar(taps_dx[:], taps_dx[:], 0.5, None, ALU.mult))
            for o in range(2):
                for dx in range(3):
                    b = band[:, 3 * o + dx]
                    tap = lambda dy: taps[:, 9 * o + 3 * dy + dx:9 * o + 3 * dy + dx + 1]
                    then(w.tensor_scalar(b, shift3[:, 0], tap(0), None, ALU.mult))
                    for dy in (1, 2):
                        then(w.scalar_tensor_tensor(b, shift3[:, dy], tap(dy), b, ALU.mult, ALU.add))
                for side in range(2):
                    n = 3 * o + 2 * side
                    then(w.tensor_scalar(halo_w[:, 2 * side + o], edge_hot[:, side], taps_dx[:, n:n + 1], None, ALU.mult))
            wv = w_v[:].rearrange("p f (h d) -> p (f h) d", h=NH)
            then(w.tensor_reduce(v_mean[:], wv, AX.X, ALU.add))
            then(w.tensor_scalar(v_mean[:], v_mean[:], -1.0 / DV, None, ALU.mult))
            then(w.tensor_tensor(wv, wv, view(v_mean, 0, [[1, FC * NH], [0, DV]]), ALU.add))
            w.tensor_scalar(gn_half[:], vecs[:, 14:18], 0.5, None, ALU.mult).then_inc(ready, 1)

            def take_wait(n):
                w.memset(marks[:, n:n + 1], 0.0)

            def gray_stage(u):
                dve.wait_ge(*gray_red.done(u))
                inner = view(gray, 1, [[D + 2, NT], [1, D]])
                w.scalar_tensor_tensor(inner, view(x_in, NT * D, [[D, NT], [1, D]]), GRAY[1], inner, ALU.mult, ALU.add).then_inc(gray_green.sem, 1)
                dve.wait_ge(*gray_green.done(u))
                w.scalar_tensor_tensor(inner, view(x_in, 2 * NT * D, [[D, NT], [1, D]]), GRAY[2], inner, ALU.mult, ALU.add).then_inc(gray_ready.sem, 1)

            def edge(r):
                def stage(u):
                    for o in range(2):
                        dve.wait_ge(*front.drained(u, F_EDGE(r, o)))
                    w.tensor_tensor(h_rows(u, r), xn[:, 2 * r:2 * r + 2], h_rows(u, r), ALU.add).then_inc(h_ready.sem, 1)
                return stage

            def normalise(u, x, stats, mv, rstd, out, stats_ready, mv_ready, rstd_ready, out_ready):
                for j in range(NT):
                    last = w.bn_stats(stats[:, j], x[:, j])
                last.then_inc(stats_ready.sem, 1)
                dve.wait_ge(*stats_ready.done(u))
                if exists(u, 1):
                    dve.wait_ge(*rstd_ready.done(back(u, 1)))
                take_wait(0 if stats is stats1 else 1)
                for j in range(NT):
                    last = w.bn_aggr(mv[:, j], stats[:, j])
                last.then_inc(mv_ready.sem, 1)
                dve.wait_ge(*rstd_ready.done(u))
                for j in range(NT):
                    last = w.tensor_scalar(out[:, j], x[:, j], mv[:, j, 0:1], rstd[:, 1, j:j + 1], ALU.subtract, ALU.mult)
                last.then_inc(out_ready.sem, 1)

            def front_norm(u):
                dve.wait_ge(*h_ready.done(u))
                normalise(u, sel(u, h), stats1, mv1, rstd1, xn, stats1_ready, mv1_ready, rstd1_ready, xn_ready)

            def shift(u):
                dve.wait_ge(*delta_ready.done(u))
                if exists(u, 1):
                    dve.wait_ge(*mix.filled(back(u, 1), M_V + 1))
                for f in range(FC):
                    per_image = "p (i t) -> p i t"
                    last = w.scalar_tensor_tensor(xp[:, f].rearrange(per_image, i=IMG), delta[:, f].rearrange(per_image, i=IMG), mu0(f),
                                                  sel(u, xT)[:, f, :, 1:T + 1], ALU.mult, ALU.add)
                last.then_inc(xp_ready.sem, 1)

            def mus(i):
                def stage(u):
                    for f in range(FC):
                        k = M_MUS[i] + f
                        dve.wait_ge(*mix.filled(u, k))
                        w.scalar_tensor_tensor(mixed[i % 2][:, f], mix.bank(u, k)[:], x_bias(i, f), delta[:, f],
                                               ALU.add, ALU.mult).then_inc(mix.drain(u, k), 1)
                return stage

            def g_stage(f):
                def stage(u):
                    k = M_G + f
                    dve.wait_ge(*g_tanh_ready.done(u, f + 1))
                    w.scalar_tensor_tensor(sel(u, g_silu)[:, f], sel(u, g_silu)[:, f], 1.0, mix.bank(u, k)[:], ALU.add, ALU.mult).then_inc(mix.drain(u, k), 1)
                return stage

            def diag_stage(u):
                dve.wait_ge(*mix.drained(u, M_R))
                dve.wait_ge(*mix.drained(u, M_K))
                if exists(u, 1):
                    dve.wait_ge(*scan.filled(back(u, 1), S_OUT(IMG - 1)))
                w.scalar_tensor_tensor(ruk[:], sel(u, rk)[:, 0], bonus, sel(u, rk)[:, 1], ALU.mult, ALU.mult).then_inc(ruk_ready.sem, 1)

            def level(lv):
                H = 1 << lv
                blocks = N // (2 * H)

                def decay_on(u):
                    dve.wait_ge(*scan.filled(u, S_LEVEL(lv, IMG - 1)))
                    if lv:
                        dve.wait_ge(*totals_ready.done(u, lv))
                        dve.wait_ge(*decayed.done(u, lv))
                    t, at = (sel(u, decay), 0) if lv == 0 else (totals, N - (N >> (lv - 1)))
                    k_left = view(sel(u, rk), N, [[2 * H, blocks], [1, H]])
                    w.tensor_tensor(k_left, k_left, view(t, at + 1, [[2, blocks], [0, H]]), ALU.mult)
                    r_right = view(r_heads, H, [[N, NH], [2 * H, blocks], [1, H]])
                    w.tensor_tensor(r_right, r_right, view(t, at, [[0, NH], [2, blocks], [0, H]]), ALU.mult).then_inc(decayed.sem, 1)

                def stage(u):
                    if lv == 0:
                        dve.wait_ge(*diag_set.done(u))
                    for img in range(IMG if lv < MASKED else 0):
                        k = S_LEVEL(lv, img)
                        if img == IMG - 1:
                            decay_on(u)
                        dve.wait_ge(*scan.filled(u, k))
                        runs, n = [64 // H, H], NT * NH // IMG
                        take_wait(2 + lv * IMG + img)
                        w.copy_predicated(view(A, img * n * P + H, [[P, n], [2 * H, runs[0]], [1, H]]),
                                          view(masks, lv * 64, [[0, n], [H, runs[0]], [1, H]]),
                                          view(scan.bank(u, k), 0, [[64, n], [H, runs[0]], [1, H]])).then_inc(scan.drain(u, k), 1)
                    if lv >= MASKED:
                        decay_on(u)
                return stage

            def gnorm(u):
                for img in range(IMG):
                    n = NT * NH // IMG
                    at = slice(img * n, (img + 1) * n)
                    dve.wait_ge(*o_sq_ready.done(u, img + 1))
                    if exists(u, 1):
                        dve.wait_ge(*o_rstd_ready.done(back(u, 1)))
                    w.tensor_reduce(o_var[:, 0, at], o_sq[:, img].rearrange("p (n d) -> p n d", n=n), AX.X, ALU.add).then_inc(o_sum_ready.sem, 1)
                for img in range(IMG):
                    k = S_AV(img)
                    dve.wait_ge(*o_rstd_ready.done(u, img + 1))
                    w.tensor_tensor(o_n[:, 2 * img:2 * img + 2].rearrange("p j (h d) -> p (j h) d", h=NH), scan.bank(u, k)[:].rearrange("p (n d) -> p n d", d=DV),
                                    view(o_var, 2 * NT * NH + img * n, [[1, n], [0, DV]]), ALU.mult).then_inc(scan.drain(u, k), 1)

            def scan_turn(u):
                for f in range(FC):
                    dve.wait_ge(*scan.drained(u, S_TR(f)))
                    dve.wait_ge(*mix.drained(u, M_G + f))
                    w.tensor_tensor(oT[:, f], oT[:, f], sel(u, g_silu)[:, f], ALU.mult).then_inc(oT_ready.sem, 1)

            def out_stage(u):
                if exists(u, 2):
                    dve.wait_ge(*stored.done(back(u, 2)))
                for img in range(IMG):
                    k = S_OUT(img)
                    dve.wait_ge(*scan.filled(u, k))
                    dve.wait_ge(*h_kept.done(u))
                    at = slice(2 * img, 2 * img + 2)
                    w.tensor_tensor(sel(u, h2)[:, at], scan.bank(u, k)[:].rearrange("p (j d) -> p j d", j=2), sel(u, h_keep)[:, at],
                                    ALU.add).then_inc(scan.drain(u, k), 1)

            def scan_norm(u):
                for img in range(IMG):
                    dve.wait_ge(*scan.drained(u, S_OUT(img)))
                x = sel(u, xn2)
                normalise(u, sel(u, h2), stats2, mv2, rstd2, x, stats2_ready, mv2_ready, rstd2_ready, xn2_ready)
                dve.wait_ge(*xn2_ready.done(u))
                for j in range(NT):
                    last = w.scalar_tensor_tensor(o_n[:, j], x[:, j], 1.0, f_g[:], ALU.mult, ALU.mult, accum_out=logit[:, j:j + 1])
                last.then_inc(logit_ready.sem, 1)
                dve.wait_ge(*logit_ready.done(u))
                w.tensor_scalar(sel(u, key)[:], logit[:], SAT_HI, SAT_LO, ALU.min, ALU.max).then_inc(key_ready.sem, 1)
                dve.wait_ge(*gate_exp.done(u))
                w.tensor_scalar(gate_e[:, 1], gate_e[:, 0], 1.0, None, ALU.add).then_inc(gate_sum.sem, 1)
                dve.wait_ge(*gate_sum.done(u))
                w.reciprocal(sel(u, gate)[:], gate_e[:, 1]).then_inc(gate_ready.sem, 1)

            def rank(u):
                dve.wait_ge(*depth.filled(u, D_KEY))
                dve.wait_ge(*key_ready.done(u))
                for j in range(NT):
                    keys_t = depth.bank(u, D_KEY)[:, (j // 2) * T:(j // 2 + 1) * T]
                    last = w.scalar_tensor_tensor(tie[:, j], keys_t, sel(u, key)[:, j:j + 1], earlier[:, j % 2], ALU.is_equal, ALU.mult)
                last.then_inc(tie_ready.sem, 1)
                dve.wait_ge(*tie_ready.done(u))
                for j in range(NT):
                    keys_t = depth.bank(u, D_KEY)[:, (j // 2) * T:(j // 2 + 1) * T]
                    last = w.scalar_tensor_tensor(before[:, j], keys_t, sel(u, key)[:, j:j + 1], tie[:, j], ALU.is_lt, ALU.add)
                last.then_inc(depth.drain(u, D_KEY), 1)
                dve.wait_ge(*depth.filled(u, D_RANK))
                w.tensor_scalar(slot_of[:], depth.bank(u, D_RANK)[:], slot_no[:], None, ALU.is_equal).then_inc(depth.drain(u, D_RANK), 1)

            def heads(n):
                def stage(u):
                    if n < IMG * QG:
                        k = D_SLOT["score", n]
                        dve.wait_ge(*depth.filled(u, k))
                        scores = depth.bank(u, k)[:].rearrange("p (h k) -> p h k", h=4)
                        w.tensor_reduce(peak[:, n % 2], scores, AX.X, ALU.max).then_inc(peak_ready.sem, 1)
                        dve.wait_ge(*peak_ready.done(u, n + 1))
                        w.tensor_tensor(E[n % 2][:], scores, view(peak, 4 * (n % 2), [[1, 4], [0, C]]), ALU.subtract).then_inc(depth.drain(u, k), 1)
                    if n == QG + 1:
                        values(u, 0)
                    if n == IMG * QG + 1:
                        values(u, 1)
                    m = n - 1
                    if 0 <= m < IMG * QG and m % 2 == 1:
                        k = D_SLOT["turn", m]
                        dve.wait_ge(*depth.filled(u, k))
                        w.tensor_copy(AT[:, 4 * (m % QG):4 * (m % QG) + 4], depth.bank(u, k)[:].rearrange("p (h q) -> p h q", h=4)).then_inc(depth.drain(u, k), 1)
                return stage

            def values(u, img):
                k = D_SLOT["av", img]
                dve.wait_ge(*depth.filled(u, k))
                o = depth.bank(u, k)[:, 0:HF * (DH + 1)].rearrange("p (h d) -> p h d", h=HF)
                w.reciprocal(r_sum[:], o[:, :, DH]).then_inc(sum_ready.sem, 1)
                dve.wait_ge(*sum_ready.done(u, img + 1))
                w.tensor_tensor(o_att[:, img].rearrange("p (h d) -> p h d", h=HF), o[:, :, 0:DH], view(r_sum, 0, [[1, HF], [0, DH]]),
                                ALU.mult).then_inc(depth.drain(u, k), 1)

            def scatter(u):
                dve.wait_ge(*gate_ready.done(u))
                for img in range(IMG):
                    k = D_SLOT["scatter", img]
                    dve.wait_ge(*depth.filled(u, k))
                    for t in range(2):
                        j = 2 * img + t
                        last = w.scalar_tensor_tensor(sel(u, h2)[:, j], depth.bank(u, k)[:, t * D:(t + 1) * D], sel(u, gate)[:, j:j + 1], sel(u, h2)[:, j],
                                                      ALU.mult, ALU.add)
                    last.then_inc(depth.drain(u, k), 1)

            stages = {
                (FRONT, "gray"): gray_stage, (FRONT, "edge0"): edge(0), (FRONT, "edge1"): edge(1), (FRONT, "norm"): front_norm,
                (MIX, "shift"): shift, (MIX, "g0"): g_stage(0), (MIX, "g1"): g_stage(1),
                (SCAN, "diag"): diag_stage, (SCAN, "gnorm"): gnorm, (SCAN, "o_turn"): scan_turn, (SCAN, "out"): out_stage, (SCAN, "norm"): scan_norm,
                (DEPTH, "rank"): rank, (DEPTH, "scatter"): scatter,
            }
            for i in range(NMIX):
                stages[MIX, f"mus{i}"] = mus(i)
            for lv in range(LEVELS):
                stages[SCAN, f"level{lv}"] = level(lv)
            for n in range(IMG * QG + 2):
                stages[DEPTH, f"heads{n}"] = heads(n)
            run_steps(dve, units, stages)

        @block.tensor
        def _(pe):
            mm = nc.tensor.matmul

            def enter(u, slots, k):
                if slots.reused(u, k):
                    pe.wait_ge(*slots.emptied(u, k))
                return slots.bank(u, k)

            def edge(r):
                def stage(u):
                    if r == 0:
                        pe.wait_ge(*gray_ready.done(u))
                        pe.wait_ge(*halo_ready.done(u))
                    for o in range(2):
                        out = enter(u, front, F_EDGE(r, o))
                        for dx in range(3):
                            mm(out[:], band[:, 3 * o + dx], gray[:, :, r, dx:dx + D], start=dx == 0, stop=False)
                        side = 1 - r
                        mm(out[:], halo_w[:, 2 * side + o], halo[:, side].rearrange("p i d -> p (i d)"), start=False, stop=True).then_inc(
                            front.fill(u, F_EDGE(r, o)), 1)
                return stage

            def turn4(u, slots, k, tile):
                out = enter(u, slots, k)
                for n in range(4):
                    last = nc.tensor.transpose(out[:, n * P:(n + 1) * P], tile(n), ident[:])
                last.then_inc(slots.fill(u, k), 1)

            def front_turn(u):
                pe.wait_ge(*xn_ready.done(u))
                for f in range(FC):
                    turn4(u, front, F_TR(f), lambda j: xn[:, j, f * P:(f + 1) * P])

            def project(u, k, weights, x, rows=P):
                out = enter(u, mix, k)
                for f in range(FC):
                    last = mm(out[0:rows, :], weights(f), x[:, f], start=f == 0, stop=f == FC - 1)
                last.then_inc(mix.fill(u, k), 1)

            def low_stage(u):
                pe.wait_ge(*xp_ready.done(u))
                project(u, M_LOW(0), lambda f: w_x0[:, f, 0:P], xp)
                project(u, M_LOW(1), lambda f: w_x0[:, f, P:P + R], xp, R)

            def mus(i):
                def stage(u):
                    for f in range(FC):
                        k = M_MUS[i] + f
                        out = enter(u, mix, k)
                        cols = slice(f * P, (f + 1) * P)
                        lhs, rhs = (w_x2[:, i, cols], low) if i < NMIX - 1 else (w_x2g[:, cols], low_g)
                        mm(out[:], lhs, rhs[:], start=True, stop=True).then_inc(mix.fill(u, k), 1)
                return stage

            def mixed_in(u, i):
                pe.wait_ge(*mixed_ready.done(u, FC * (i + 1)))
                return mixed[i % 2]

            def w2(u):
                pe.wait_ge(*mix.drained(u, M_W1))
                out = enter(u, mix, M_W2)
                mm(out[:], w_w2[:], w_low, start=True, stop=True).then_inc(mix.fill(u, M_W2), 1)

            def v_stage(u):
                x = mixed_in(u, 3)
                for n in range(2):
                    out = enter(u, mix, M_V + n)
                    for jj in range(2):
                        j = 2 * n + jj
                        for f in range(FC):
                            last = mm(out[:, jj * D:(jj + 1) * D], x[:, f, j * P:(j + 1) * P], w_v[:, f], start=f == 0, stop=f == FC - 1)
                    last.then_inc(mix.fill(u, M_V + n), 1)

            def diag_stage(u):
                pe.wait_ge(*ruk_ready.done(u))
                out = enter(u, scan, S_DIAG)
                for j in range(NT):
                    last = mm(out[:, j * NH:(j + 1) * NH], ruk[:, j * P:(j + 1) * P], head_of[:], start=True, stop=True)
                last.then_inc(scan.fill(u, S_DIAG), 1)

            def level(lv):
                H = 1 << lv

                def stage(u):
                    rk_u = sel(u, rk)
                    if lv:
                        pe.wait_ge(*decayed.done(u, lv))
                    else:
                        pe.wait_ge(*r_heads_ready.done(u))
                        pe.wait_ge(*mix.drained(u, M_K))
                    for img in range(IMG):
                        k = S_LEVEL(lv, img)
                        out = enter(u, scan, k)
                        if lv == LEVELS:
                            at = img * T
                            last = mm(out[:], rk_u[:, 1, at:at + P], r_heads[:, :, at + P:at + T], start=True, stop=True)
                        else:
                            for t in range(2):
                                at = img * T + t * P
                                right = view(r_heads, at + H, [[N, NH], [2 * H, 64 // H], [1, H]])
                                last = mm(out[:, t * T:(t + 1) * T], rk_u[:, 1, at:at + P], right, start=True, stop=True)
                        last.then_inc(scan.fill(u, k), 1)
                return stage

            def av(u):
                for n in range(2):
                    pe.wait_ge(*mix.drained(u, M_V + n))
                pe.wait_ge(*scan.drained(u, S_LEVEL(LEVELS, IMG - 1)))
                for img in range(IMG):
                    k = S_AV(img)
                    out = enter(u, scan, k)
                    for t in range(2):
                        for hh in range(NH):
                            dst = out[:, t * D + hh * DV:t * D + (hh + 1) * DV]
                            vals = lambda j: sel(u, v)[:, j, hh * DV:(hh + 1) * DV]
                            last = mm(dst, A[:, (2 * img + t) * NH + hh], vals(2 * img + t), start=True, stop=t == 0)
                            if t:
                                last = mm(dst, A_far[:, img * NH + hh], vals(2 * img), start=False, stop=True)
                    last.then_inc(scan.fill(u, k), 1)

            def scan_turn(u):
                pe.wait_ge(*scan.drained(u, S_AV(1)))
                for f in range(FC):
                    turn4(u, scan, S_TR(f), lambda j: o_n[:, j, f * P:(f + 1) * P])

            def out_stage(u):
                pe.wait_ge(*oT_ready.done(u))
                for img in range(IMG):
                    out = enter(u, scan, S_OUT(img))
                    for t in range(2):
                        j = 2 * img + t
                        for f in range(FC):
                            last = mm(out[:, t * D:(t + 1) * D], oT[:, f, j * P:(j + 1) * P], w_o[:, f], start=f == 0, stop=f == FC - 1)
                    last.then_inc(scan.fill(u, S_OUT(img)), 1)

            def key_stage(u):
                pe.wait_ge(*key_ready.done(u))
                turn4(u, depth, D_KEY, lambda j: view(sel(u, key), j, [[0, P]]))

            def rank(u):
                pe.wait_ge(*depth.drained(u, D_KEY))
                out = enter(u, depth, D_RANK)
                for img in range(IMG):
                    for t in range(2):
                        last = mm(out[:, img * T:(img + 1) * T], ones_bf[:], before[:, 2 * img + t], start=t == 0, stop=t == 1)
                last.then_inc(depth.fill(u, D_RANK), 1)

            def pick_stage(u):
                pe.wait_ge(*depth.drained(u, D_RANK))
                turn4(u, depth, D_PICK, lambda j: slot_of[:, j * P:(j + 1) * P])

            def select(u):
                pe.wait_ge(*depth.drained(u, D_PICK))
                pe.wait_ge(*xn2_ready.done(u))
                out = enter(u, depth, D_SEL)
                for c in range(FC):
                    for img in range(IMG):
                        for t in range(2):
                            j = 2 * img + t
                            last = mm(out[:, (c * IMG + img) * C:(c * IMG + img + 1) * C], sel(u, xn2)[:, j, c * P:(c + 1) * P], pick[:, j], start=t == 0, stop=t == 1)
                last.then_inc(depth.fill(u, D_SEL), 1)

            def qkv(u):
                pe.wait_ge(*depth.drained(u, D_SEL))
                n = IMG * C
                for k, weights in ((D_Q, f_q), (D_K, f_k)):
                    out = enter(u, depth, k)
                    for c in range(FC):
                        for f in range(FC):
                            last = mm(out[:, c * n:(c + 1) * n], weights[:, f, c * P:(c + 1) * P], selT[:, f], start=f == 0, stop=f == FC - 1)
                    last.then_inc(depth.fill(u, k), 1)
                out = enter(u, depth, D_V)
                for img in range(IMG):
                    for f in range(FC):
                        last = mm(out[:, img * D:(img + 1) * D], selT[:, f, img * C:(img + 1) * C], f_v[:, f], start=f == 0, stop=f == FC - 1)
                last.then_inc(depth.fill(u, D_V), 1)

            def values(u, img):
                if img:
                    pe.wait_ge(*depth.drained(u, D_SLOT["turn", IMG * QG - 1]))
                k = D_SLOT["av", img]
                out = enter(u, depth, k)
                for g in range(QG):
                    for hh in range(4):
                        head = 8 * (hh // 2) + 2 * g + hh % 2
                        last = mm(out[:, head * (DH + 1):(head + 1) * (DH + 1)], AT[:, 4 * g + hh], vA[:, img * HF + head], start=True, stop=True)
                last.then_inc(depth.fill(u, k), 1)

            def heads(n):
                def stage(u):
                    if n < IMG * QG:
                        img, g = divmod(n, QG)
                        out = enter(u, depth, D_SLOT["score", n])
                        for hh in range(4):
                            c, pair, odd = hh // 2, g, hh % 2
                            rows, cols = slice(32 * pair, 32 * pair + 32), slice(img * C, (img + 1) * C)
                            last = mm(out[:, hh * C:(hh + 1) * C], q_par[odd][rows, c, cols], kT[rows, c, cols], start=True, stop=True)
                        last.then_inc(depth.fill(u, D_SLOT["score", n]), 1)
                    if n == QG + 1:
                        values(u, 0)
                    if n == IMG * QG + 1:
                        values(u, 1)
                    m = n - 1
                    if 0 <= m < IMG * QG:
                        pe.wait_ge(*exp_ready.done(u, m + 1))
                        turn4(u, depth, D_SLOT["turn", m], lambda hh: E[m % 2][:, hh])
                return stage

            def depth_turn(u):
                pe.wait_ge(*depth.drained(u, D_SLOT["av", 1]))
                turn4(u, depth, D_SLOT["o_turn"], lambda n: o_att[:, n % IMG, (n // IMG) * P:(n // IMG + 1) * P])

            def y_stage(u):
                pe.wait_ge(*depth.drained(u, D_SLOT["o_turn"]))
                out = enter(u, depth, D_SLOT["y"])
                for img in range(IMG):
                    for c in range(FC):
                        last = mm(out[:, img * D:(img + 1) * D], o_attT[:, c, img * C:(img + 1) * C], f_o[:, c], start=c == 0, stop=c == FC - 1)
                last.then_inc(depth.fill(u, D_SLOT["y"]), 1)

            def scatter(u):
                pe.wait_ge(*depth.drained(u, D_SLOT["y"]))
                for img in range(IMG):
                    k = D_SLOT["scatter", img]
                    out = enter(u, depth, k)
                    for t in range(2):
                        at = (2 * img + t) * P
                        last = mm(out[:, t * D:(t + 1) * D], slot_of[:, at:at + P], y[:, img], start=True, stop=True)
                    last.then_inc(depth.fill(u, k), 1)

            stages = {
                (FRONT, "edge0"): edge(0), (FRONT, "edge1"): edge(1), (FRONT, "turn"): front_turn,
                (MIX, "low"): low_stage, (MIX, "w2"): w2, (MIX, "v"): v_stage,
                (MIX, "r"): lambda u: project(u, M_R, lambda f: w_r[:, f], mixed_in(u, 0)),
                (MIX, "w1"): lambda u: project(u, M_W1, lambda f: w_w1[:, f], mixed_in(u, 1), GLR),
                (MIX, "k"): lambda u: project(u, M_K, lambda f: w_k[:, f], mixed_in(u, 2)),
                (MIX, "g0"): lambda u: project(u, M_G, lambda f: w_g[:, f, 0:P], mixed_in(u, 4)),
                (MIX, "g1"): lambda u: project(u, M_G + 1, lambda f: w_g[:, f, P:D], mixed_in(u, 4)),
                (SCAN, "diag"): diag_stage, (SCAN, "av"): av, (SCAN, "o_turn"): scan_turn, (SCAN, "out"): out_stage,
                (DEPTH, "key"): key_stage, (DEPTH, "rank"): rank, (DEPTH, "pick"): pick_stage, (DEPTH, "select"): select, (DEPTH, "qkv"): qkv,
                (DEPTH, "o_turn"): depth_turn, (DEPTH, "y"): y_stage, (DEPTH, "scatter"): scatter,
            }
            for i in range(NMIX):
                stages[MIX, f"mus{i}"] = mus(i)
            for lv in range(LEVELS + 1):
                stages[SCAN, f"level{lv}"] = level(lv)
            for n in range(IMG * QG + 2):
                stages[DEPTH, f"heads{n}"] = heads(n)
            pe.wait_ge(consts, ALL_CONSTS)
            pe.wait_ge(zeroed, PADS)
            pe.wait_ge(ready, 1)
            run_steps(pe, units, stages)


def shape_constants():
    k, m = np.arange(P)[:, None], np.arange(P)[None, :]
    shift3 = np.stack([k == m + dy - 1 for dy in range(3)], 1).astype(np.float32)
    edge_hot = np.zeros((3, 2, P), np.float32)
    edge_hot[:, 0, 0] = 1
    edge_hot[:, 1, P - 1] = 1
    masks = np.zeros((P, MASKED, 64), np.int32)
    for lv in range(MASKED):
        H, c = 1 << lv, np.arange(64)
        left = c // H * 2 * H
        masks[:, lv] = (k >= left) & (k < left + H)
    s, t = np.arange(T)[:, None], np.arange(T)[None, :]
    earlier = (s < t).astype(np.float32).reshape(2, P, T).transpose(1, 0, 2)
    p = np.arange(P)
    parity = np.stack([(p // DH % 2 == n) / DH ** 0.5 for n in range(2)], 1).astype(np.float32)
    return {
        "ident": np.eye(P, dtype=np.float32), "shift3": shift3, "edge_hot": edge_hot, "masks": masks, "earlier": np.ascontiguousarray(earlier),
        "slot_no": p[:, None].astype(np.float32), "head_of": (p[:, None] // DK == np.arange(NH)).astype(np.float32), "parity": parity,
    }


def lay_out(x, L0_tok_scharr, L0_attn_mu0, L0_attn_W_x0, L0_attn_W_x2, L0_attn_x_bias, L0_attn_W_r, L0_attn_W_w1, L0_attn_W_w2, L0_attn_b_w2,
            L0_attn_W_k, L0_attn_W_v, L0_attn_W_g, L0_attn_bonus, L0_attn_gn_weight, L0_attn_gn_bias, L0_attn_W_o, L0_ffn_Wg, L0_ffn_Wq,
            L0_ffn_Wk, L0_ffn_Wv, L0_ffn_Wo):
    chunks = lambda w: np.asarray(w).reshape(FC, P, -1).transpose(1, 0, 2)
    cols = lambda b: np.asarray(b).reshape(-1, P).T
    scharr, w_x2 = np.asarray(L0_tok_scharr), np.asarray(L0_attn_W_x2).T
    by_path = np.zeros((P, NMIX, D), w_x2.dtype)
    for i in range(NMIX):
        rows = i * R % P
        by_path[rows:rows + R, i] = w_x2[i * R:(i + 1) * R]
    return {
        "x": np.asarray(x),
        "taps": np.broadcast_to(scharr.reshape(1, 18), (P, 18)),
        "taps_dx": scharr.reshape(6, 3).T,
        "w_x0": chunks(np.asarray(L0_attn_W_x0).T), "w_x2": by_path[:, 0:NMIX - 1], "w_x2g": by_path[:, NMIX - 1],
        "vecs": np.concatenate([cols(L0_attn_mu0), cols(L0_attn_x_bias), cols(L0_attn_b_w2), cols(L0_attn_bonus), cols(L0_attn_gn_weight),
                                cols(L0_attn_gn_bias)], 1),
        "w_r": chunks(np.asarray(L0_attn_W_r).T), "w_w1": chunks(np.asarray(L0_attn_W_w1).T), "w_w2": np.asarray(L0_attn_W_w2).T,
        "w_k": chunks(np.asarray(L0_attn_W_k).T), "w_v": chunks(np.asarray(L0_attn_W_v).T), "w_g": chunks(np.asarray(L0_attn_W_g).T),
        "w_o": chunks(np.asarray(L0_attn_W_o).T),
        "f_g": np.broadcast_to(np.asarray(L0_ffn_Wg).reshape(1, D), (P, D)), "f_q": chunks(L0_ffn_Wq), "f_k": chunks(L0_ffn_Wk),
        "f_v": chunks(L0_ffn_Wv), "f_o": chunks(L0_ffn_Wo),
    }


def kernel(**inputs):
    import concourse.bacc as bacc
    from concourse.bass_utils import run_bass_kernel_spmd

    nc = bacc.Bacc("TRN2", target_bir_lowering=False, num_devices=1)
    arrays = {n: np.ascontiguousarray(v) for n, v in {**lay_out(**inputs), **shape_constants()}.items()}
    images = arrays["x"].shape[0]
    aps = {n: nc.dram_tensor(f"in_{n}", v.shape, mybir.dt.from_np(v.dtype), kind="ExternalInput").ap() for n, v in arrays.items()}
    aps["out"] = nc.dram_tensor("out_h", (images, T, D), F32, kind="ExternalOutput").ap()
    build(nc, aps, images // IMG)
    r = run_bass_kernel_spmd(nc, [{f"in_{n}": v for n, v in arrays.items()}], core_ids=[0])
    return r.results[0]["out_h"]
```
